# Optimizing a Trainium2 kernel written in Bass

```python
import numpy as np
import jax
import jax.numpy as jnp

def _softmax(x, axis=-1):
    return jax.nn.softmax(x, axis=axis)
def _gelu(x):
    return jax.nn.gelu(x, approximate=True)
def _silu(x):
    return jax.nn.silu(x)
def _sigmoid(x):
    return jax.nn.sigmoid(x)
def _layernorm(x, axis=-1, eps=1e-5):
    m = jnp.mean(x, axis=axis, keepdims=True)
    v = jnp.var(x, axis=axis, keepdims=True)
    return (x - m) / jnp.sqrt(v + eps)
def _scatter_add(tgt, idx, src, axis=0):
    return tgt.at[idx].add(src)
def _segment_sum(src, seg, n):
    return jax.ops.segment_sum(src, seg, n)

kernel_name = 'mk_conv_preact_d1_conv_nchw8_9882b9'

def setup_inputs(seed: int = 0):
    np.random.seed(seed)
    _w = jnp.asarray
    def _rec_inputs():
        import jax
        import jax.numpy as jnp
        _gk = jax.random.key(seed)
        x = -0.000125 + 0.9999 * jax.random.normal(jax.random.fold_in(_gk, 1), (32, 8, 256, 512), jnp.float32)
        return x
    x = _rec_inputs()
    def _L0_conv_setup():
        import jax, jax.numpy as jnp
        import numpy as np
        T, B, N, D = (32, 8, 256, 512)
        TAU = 2.0
        VTH = 1.0
        ALPHA = 4.0

        def _spike(v):
            s = jax.nn.sigmoid(ALPHA * v)
            return s + jax.lax.stop_gradient((v > 0).astype(v.dtype) - s)
        key = jax.random.key(seed)
        k0, k1, k2 = jax.random.split(key, 3)
        scale = 1.0 / np.sqrt(D)
        return {'x': jax.random.normal(k0, (T, B, N, D), jnp.float32), 'tr_mx': jnp.zeros((B, N, D), jnp.float32), 'W_lif': jax.random.normal(k1, (D, D), jnp.float32) * scale, 'b_lif': jnp.zeros((D,), jnp.float32), 'W_rec': jax.random.normal(k2, (D, D), jnp.float32) * scale, 'b_rec': jnp.zeros((D,), jnp.float32)}
    _L0_conv_all = _L0_conv_setup()
    _L0_conv_in = {k: v for k, v in _L0_conv_all.items() if k in ('tr_mx', 'W_lif', 'b_lif', 'W_rec', 'b_rec', )}
    del _L0_conv_all

    return {
        "x": x,
        "L0_conv_tr_mx": _L0_conv_in["tr_mx"],
        "L0_conv_W_lif": _L0_conv_in["W_lif"],
        "L0_conv_b_lif": _L0_conv_in["b_lif"],
        "L0_conv_W_rec": _L0_conv_in["W_rec"],
        "L0_conv_b_rec": _L0_conv_in["b_rec"],
    }

def reference(x, L0_conv_tr_mx, L0_conv_W_lif, L0_conv_b_lif, L0_conv_W_rec, L0_conv_b_rec):
    import jax
    import jax.numpy as jnp
    def _L0_conv_ref(x, tr_mx, W_lif, b_lif, W_rec, b_rec):
        import jax, jax.numpy as jnp
        import numpy as np
        T, B, N, D = (32, 8, 256, 512)
        TAU = 2.0
        VTH = 1.0
        ALPHA = 4.0

        def _spike(v):
            s = jax.nn.sigmoid(ALPHA * v)
            return s + jax.lax.stop_gradient((v > 0).astype(v.dtype) - s)
        inp = jnp.einsum('tbnd,de->tbne', x, W_lif) + b_lif

        def step(mem, i_t):
            mem = mem + (i_t - mem) / TAU
            sp = _spike(mem - VTH)
            mem = mem * (1.0 - sp)
            return (mem, sp)
        _, sp_seq = jax.lax.scan(step, tr_mx, inp)
        g = x * (1.0 - sp_seq)
        rec_x = jnp.einsum('tbnd,dp->tbnp', g, W_rec) + b_rec
        return rec_x

    def _gn(v, G=4, eps=1e-5):
        B_, C_, H_, W_ = v.shape
        g = v.reshape(B_, G, C_ // G, H_, W_)
        m = jnp.mean(g, axis=(2, 3, 4), keepdims=True)
        s = jnp.var(g, axis=(2, 3, 4), keepdims=True)
        return ((g - m) / jnp.sqrt(s + eps)).reshape(v.shape)

    def _ln_c(v, eps=1e-6):
        m = jnp.mean(v, axis=1, keepdims=True)
        s = jnp.var(v, axis=1, keepdims=True)
        return (v - m) / jnp.sqrt(s + eps)

    def _ln_t(v, eps=1e-5):
        m = jnp.mean(v, axis=-1, keepdims=True)
        s = jnp.var(v, axis=-1, keepdims=True)
        return (v - m) / jnp.sqrt(s + eps)

    def _to_tokens(v):
        B_, C_, H_, W_ = v.shape
        return v.reshape(B_, C_, H_ * W_).transpose(0, 2, 1)
    def _from_tokens(t, like):
        B_, C_, H_, W_ = like.shape
        return t.transpose(0, 2, 1).reshape(B_, C_, H_, W_)

    x = x + _L0_conv_ref(_gn(x), L0_conv_tr_mx, L0_conv_W_lif, L0_conv_b_lif, L0_conv_W_rec, L0_conv_b_rec)
    return x


_drawn_inputs = setup_inputs


def setup_inputs(seed=0):
    import zlib

    import numpy as np

    out = dict(_drawn_inputs(seed))
    spreads = {'L0_conv_tr_mx': (0.0, 0.587), 'L0_conv_b_lif': (0.0, 0.1), 'L0_conv_b_rec': (0.0, 0.1)}
    factors = {}
    for name, (base, spread) in spreads.items():
        noise = np.random.default_rng([zlib.crc32(name.encode()), seed]).standard_normal(out[name].shape)
        drawn = base * np.exp(spread * noise) if base else spread * noise
        out[name] = jnp.asarray(drawn.astype(out[name].dtype))
    for name, factor in factors.items():
        out[name] = (out[name] * factor).astype(out[name].dtype)
    return out
```

```python
from contextlib import ExitStack

import concourse.bass as bass
from concourse import mybir

P = 128
BANK = 512


def lif_block(nc: bass.Bass, x, tr_mx, w_lif, b_lif, w_rec, b_rec, out):
    f32 = mybir.dt.float32
    f32r = mybir.dt.float32r
    ALU = mybir.AluOpType
    ACT = mybir.ActivationFunctionType

    T, B, N, D = x.shape
    GROUPS = 4
    R = B // GROUPS * N
    TPP = R // P
    C = D // P
    S = T * GROUPS
    EPS = 1e-5
    SLOTS = 8
    AHEAD = 4
    assert R == BANK and D == BANK and TPP == C == GROUPS == 4 and 2 * GROUPS == SLOTS

    x_steps = x.rearrange("t b n d -> (t b n d)").rearrange("(s p j d) -> s p j d", p=P, j=TPP, d=D)
    out_steps = out.rearrange("t b n d -> (t b n d)").rearrange("(s p j d) -> s p j d", p=P, j=TPP, d=D)
    mem_groups = tr_mx.rearrange("b n d -> (b n d)").rearrange("(g p j d) -> g p j d", p=P, j=TPP, d=D)
    w_lif_chunks = w_lif.rearrange("(k p) e -> p k e", p=P)
    w_rec_chunks = w_rec.rearrange("(k p) e -> p k e", p=P)

    with ExitStack() as ctx:
        def sb(name, shape, dt=f32):
            return ctx.enter_context(nc.sbuf_tensor(name, shape, dt))

        def pb(name):
            return ctx.enter_context(nc.psum_tensor(name, [P, BANK], f32))

        def sem(name):
            return ctx.enter_context(nc.semaphore(name))

        x_ring = [sb(f"x_ring{i}", [P, TPP, D]) for i in range(SLOTS)]
        xn = sb("xn", [P, TPP, D])
        xT = [sb(f"xT{i}", [P, 2, C, R], f32r) for i in range(2)]
        gated = [sb(f"gated{i}", [P, 2, C, R], f32r) for i in range(2)]
        state = [sb(f"state{g}", [P, C, R]) for g in range(GROUPS)]
        u_buf = [sb(f"u{i}", [P, R]) for i in range(2)]
        wl = sb("wl", [P, 2, C, D], f32r)
        wr = sb("wr", [P, 2, C, D], f32r)
        b_rec_bc = sb("b_rec_bc", [P, D])
        b_lif_col = sb("b_lif_col", [P, C])
        ident = sb("ident", [P, P])
        averaging = sb("averaging", [P, P])
        minus_half = sb("minus_half", [P, 1])
        sums = sb("sums", [P, 2])
        squares = sb("squares", [P, 2])
        neg_mean = sb("neg_mean", [P, 2])
        var_eps = sb("var_eps", [P, 2])
        rstd = sb("rstd", [P, 2])
        shift = sb("shift", [P, 2])

        tp_ps = [pb(f"tp_ps{i}") for i in range(2)]
        y_ps = [pb(f"y_ps{i}") for i in range(2)]
        r_ps = [pb(f"r_ps{i}") for i in range(2)]
        stat_ps = pb("stat_ps")
        mem_ps = pb("mem_ps")

        x_loaded = [sem(f"x_loaded{i}") for i in range(SLOTS)]
        out_stored = [sem(f"out_stored{i}") for i in range(SLOTS)]
        w_lif_loaded = sem("w_lif_loaded")
        w_rec_loaded = sem("w_rec_loaded")
        biases_loaded = sem("biases_loaded")
        mem_loaded = [sem(f"mem_loaded{g}") for g in range(GROUPS)]
        zeros_ready = sem("zeros_ready")
        ident_ready = sem("ident_ready")
        averaging_ready = sem("averaging_ready")
        half_ready = sem("half_ready")
        wl_hi_ready = sem("wl_hi_ready")
        wl_ready = sem("wl_ready")
        wr_hi_ready = sem("wr_hi_ready")
        wr_ready = sem("wr_ready")
        mem_transposed = sem("mem_transposed")
        sum_ready = sem("sum_ready")
        mean_ready = sem("mean_ready")
        neg_mean_ready = sem("neg_mean_ready")
        squares_ready = sem("squares_ready")
        var_ready = sem("var_ready")
        var_eps_ready = sem("var_eps_ready")
        rstd_ready = sem("rstd_ready")
        shift_ready = sem("shift_ready")
        xn_ready = sem("xn_ready")
        residual_ready = sem("residual_ready")
        chunk_transposed = sem("chunk_transposed")
        hi_ready = sem("hi_ready")
        lo_ready = sem("lo_ready")
        y_ready = sem("y_ready")
        u_ready = sem("u_ready")
        gated_ready = sem("gated_ready")
        reset_done = sem("reset_done")
        state_ready = sem("state_ready")
        r_ready = sem("r_ready")
        out_ready = sem("out_ready")

        block = ctx.enter_context(nc.Block())

        LOOP_FIRST = 4
        LOOP_END = (S - LOOP_FIRST) // SLOTS * SLOTS
        LAST_Q = S - LOOP_END

        def has(b, q, d):
            return not isinstance(b, int) or 0 <= b + q + d < S

        def dma_count(b, q):
            return b * (16 // SLOTS) + 16 * (q // SLOTS + 1)

        @block.sync
        def _(sp):
            def load(b, q):
                sp.dma_start(x_ring[q % SLOTS][:], x_steps[b + q]).then_inc(x_loaded[q % SLOTS], 16)

            def store(b, q):
                sp.wait_ge(out_ready, (b + q) * TPP + TPP)
                sp.dma_start(out_steps[b + q], x_ring[q % SLOTS][:]).then_inc(out_stored[q % SLOTS], 16)

            load(0, 0)
            sp.dma_start(x_ring[7][:], w_lif_chunks).then_inc(w_lif_loaded, 16)
            sp.dma_start(b_lif_col[:], b_lif.rearrange("(c p) -> p c", p=P), allow_slow_non_contiguous=True).then_inc(biases_loaded, 16)
            sp.dma_start(b_rec_bc[:], b_rec.partition_broadcast(P)).then_inc(biases_loaded, 16)
            sp.dma_start(x_ring[4][:], mem_groups[0]).then_inc(mem_loaded[0], 16)
            load(0, 1)
            sp.dma_start(x_ring[6][:], w_rec_chunks).then_inc(w_rec_loaded, 16)
            sp.dma_start(x_ring[5][:], mem_groups[1]).then_inc(mem_loaded[1], 16)
            load(0, 2)
            sp.wait_ge(wl_ready, 1)
            sp.dma_start(x_ring[7][:], mem_groups[2]).then_inc(mem_loaded[2], 16)
            sp.wait_ge(wr_ready, 1)
            sp.dma_start(x_ring[6][:], mem_groups[3]).then_inc(mem_loaded[3], 16)
            load(0, 3)
            sp.wait_ge(mem_transposed, C)
            load(0, 4)
            sp.wait_ge(mem_transposed, 2 * C)
            load(0, 5)
            store(0, 0)
            sp.wait_ge(mem_transposed, GROUPS * C)
            load(0, 6)
            store(0, 1)
            load(0, 7)
            store(0, 2)

            def step(b, q):
                if has(b, q, AHEAD):
                    sp.wait_ge(out_stored[(q + AHEAD) % SLOTS], dma_count(b, q + AHEAD - SLOTS))
                    load(b, q + AHEAD)
                store(b, q - 1)

            with sp.Fori(0, LOOP_END // SLOTS) as i:
                b = i * SLOTS
                for q in range(LOOP_FIRST, LOOP_FIRST + SLOTS):
                    step(b, q)
            for q in range(LOOP_FIRST, LAST_Q + 1):
                step(LOOP_END, q)
            for i in range(SLOTS):
                sp.wait_ge(out_stored[i], 16 * (S // SLOTS))

        @block.gpsimd
        def _(pool):
            nc.gpsimd.memset(ident[:], 0.0).then_inc(zeros_ready, 1)
            nc.gpsimd.memset(averaging[:], 1.0 / (R * D)).then_inc(averaging_ready, 1)
            nc.gpsimd.memset(minus_half[:], -0.5).then_inc(half_ready, 1)
            pool.wait_ge(zeros_ready, 1)
            nc.gpsimd.affine_select(out=ident[:], in_=ident[:], compare_op=ALU.not_equal, fill=1.0, base=0,
                                    pattern=[[-1, P]], channel_multiplier=1).then_inc(ident_ready, 1)
            pool.wait_ge(half_ready, 1)
            pool.wait_ge(biases_loaded, 32)

            def step(b, q):
                if has(b, q, 1):
                    slot = x_ring[(q + 1) % SLOTS]
                    pool.wait_ge(xn_ready, b + q + 2)
                    nc.gpsimd.tensor_tensor(slot[:], slot[:], b_rec_bc[:].unsqueeze(1).broadcast_to([P, TPP, D]),
                                            ALU.add).then_inc(residual_ready, 1)
                if has(b, q, 2):
                    par = q % 2
                    pool.wait_ge(var_eps_ready, b + q + 3)
                    nc.gpsimd.tensor_tensor(rstd[:, par:par + 1], var_eps[:, par:par + 1], minus_half[:],
                                            ALU.pow).then_inc(rstd_ready, 1)

            for q in range(-2, LOOP_FIRST):
                step(0, q)
            with pool.Fori(0, LOOP_END // SLOTS) as i:
                b = i * SLOTS
                for q in range(LOOP_FIRST, LOOP_FIRST + SLOTS):
                    step(b, q)
            for q in range(LOOP_FIRST, LAST_Q + 1):
                step(LOOP_END, q)

        @block.scalar
        def _(act):
            def hi_part(b, q, c):
                act.wait_ge(chunk_transposed, (b + q) * C + c + 1)
                nc.scalar.activation(xT[q % 2][:, 0, c, :], tp_ps[c % 2][:], ACT.Copy).then_inc(hi_ready, 1)

            def total(b, q):
                act.wait_ge(x_loaded[q % SLOTS], dma_count(b, q))
                nc.scalar.activation(xn[:], x_ring[q % SLOTS][:], ACT.Copy,
                                     accum_out=sums[:, q % 2:q % 2 + 1]).then_inc(sum_ready, 1)

            def deviations(b, q):
                par = slice(q % 2, q % 2 + 1)
                act.wait_ge(mean_ready, b + q + 1)
                nc.scalar.activation(neg_mean[:, par], stat_ps[:, 0:1], ACT.Copy, scale=-1.0).then_inc(neg_mean_ready, 1)
                act.wait_ge(neg_mean_ready, b + q + 1)
                nc.scalar.activation(xn[:], x_ring[q % SLOTS][:], ACT.Square, bias=neg_mean[:, par],
                                     accum_out=squares[:, par]).then_inc(squares_ready, 1)

            def normalise(b, q):
                par = slice(q % 2, q % 2 + 1)
                act.wait_ge(rstd_ready, b + q + 1)
                nc.scalar.activation(shift[:, par], neg_mean[:, par], ACT.Copy,
                                     scale=rstd[:, par]).then_inc(shift_ready, 1)
                act.wait_ge(shift_ready, b + q + 1)
                nc.scalar.activation(xn[:], x_ring[q % SLOTS][:], ACT.Identity, bias=shift[:, par],
                                     scale=rstd[:, par]).then_inc(xn_ready, 1)

            def halve(b, q, e):
                act.wait_ge(reset_done, (b + q) * C + e + 1)
                st = state[q % GROUPS][:, e, :]
                nc.scalar.activation(st, st, ACT.Identity, bias=b_lif_col[:, e:e + 1], scale=0.5).then_inc(state_ready, 1)

            def first_state(g):
                for e in range(C):
                    act.wait_ge(mem_transposed, g * C + e + 1)
                    nc.scalar.activation(state[g][:, e, :], mem_ps[:], ACT.Identity,
                                         bias=b_lif_col[:, e:e + 1]).then_inc(state_ready, 1)

            def step(b, q):
                if has(b, q, 1):
                    if has(b, q, -1):
                        act.wait_ge(gated_ready, (b + q) * C)
                    for c in range(C):
                        hi_part(b, q + 1, c)
                if has(b, q, 2):
                    if has(b, q, 1):
                        act.wait_ge(chunk_transposed, (b + q + 2) * C)
                    total(b, q + 2)
                if has(b, q, -1):
                    halve(b, q - 1, 0)
                    halve(b, q - 1, 1)
                if has(b, q, 2):
                    deviations(b, q + 2)
                if has(b, q, -1):
                    halve(b, q - 1, 2)
                    halve(b, q - 1, 3)
                if has(b, q, 2):
                    normalise(b, q + 2)

            step(0, -2)
            act.wait_ge(biases_loaded, 32)
            first_state(0)
            step(0, -1)
            first_state(1)
            step(0, 0)
            first_state(2)
            first_state(3)
            for q in range(1, LOOP_FIRST):
                step(0, q)
            with act.Fori(0, LOOP_END // SLOTS) as i:
                b = i * SLOTS
                for q in range(LOOP_FIRST, LOOP_FIRST + SLOTS):
                    step(b, q)
            for q in range(LOOP_FIRST, LAST_Q + 1):
                step(LOOP_END, q)

        @block.vector
        def _(dve):
            def split_weight(raw, parts, loaded, hi_sem, both_sem):
                dve.wait_ge(loaded, 16)
                nc.vector.tensor_copy(parts[:, 0], raw[:]).then_inc(hi_sem, 1)
                dve.wait_ge(hi_sem, 1)
                nc.vector.tensor_tensor(parts[:, 1], raw[:], parts[:, 0].bitcast(f32), ALU.subtract).then_inc(both_sem, 1)

            def lo_part(b, q, c):
                dve.wait_ge(hi_ready, (b + q) * C + c + 1)
                nc.vector.tensor_tensor(xT[q % 2][:, 1, c, :], tp_ps[c % 2][:], xT[q % 2][:, 0, c, :].bitcast(f32),
                                        ALU.subtract).then_inc(lo_ready, 1)

            def spike(b, q, e):
                n = (b + q) * C + e + 1
                u, st = u_buf[e % 2], state[q % GROUPS][:, e, :]
                dve.wait_ge(y_ready, n)
                dve.wait_ge(state_ready, n)
                nc.vector.tensor_tensor(u[:], y_ps[e % 2][:], st, ALU.add).then_inc(u_ready, 1)
                dve.wait_ge(u_ready, n)
                nc.vector.scalar_tensor_tensor(gated[q % 2][:, :, e, :], u[:].unsqueeze(1).broadcast_to([P, 2, R]), 2.0,
                                               xT[q % 2][:, :, e, :].bitcast(f32), ALU.is_le, ALU.mult).then_inc(gated_ready, 1)
                nc.vector.scalar_tensor_tensor(st, u[:], 2.0, u[:], ALU.is_le, ALU.mult).then_inc(reset_done, 1)

            def output(b, q, j):
                dve.wait_ge(r_ready, (b + q) * TPP + j + 1)
                if j == 0:
                    dve.wait_ge(residual_ready, b + q + 1)
                rows = x_ring[q % SLOTS][:, j, :]
                nc.vector.tensor_tensor(rows, r_ps[j % 2][:], rows, ALU.add).then_inc(out_ready, 1)

            def add_eps(b, q):
                dve.wait_ge(var_ready, b + q + 1)
                nc.vector.tensor_scalar(var_eps[:, q % 2:q % 2 + 1], stat_ps[:, 1:2], EPS, None,
                                        ALU.add).then_inc(var_eps_ready, 1)

            def step(b, q):
                for part in range(4):
                    if has(b, q, 1) and part < 2:
                        lo_part(b, q + 1, 2 * part)
                        lo_part(b, q + 1, 2 * part + 1)
                    if has(b, q, 0):
                        spike(b, q, part)
                    if has(b, q, 2) and part == 2:
                        add_eps(b, q + 2)
                    if has(b, q, -1):
                        output(b, q - 1, part)

            split_weight(x_ring[7], wl, w_lif_loaded, wl_hi_ready, wl_ready)
            step(0, -2)
            split_weight(x_ring[6], wr, w_rec_loaded, wr_hi_ready, wr_ready)
            for q in range(-1, LOOP_FIRST):
                step(0, q)
            with dve.Fori(0, LOOP_END // SLOTS) as i:
                b = i * SLOTS
                for q in range(LOOP_FIRST, LOOP_FIRST + SLOTS):
                    step(b, q)
            for q in range(LOOP_FIRST, LAST_Q + 1):
                step(LOOP_END, q)

        @block.tensor
        def _(pe):
            def transpose_chunk(b, q, c):
                n = (b + q) * C + c
                if c == 0:
                    pe.wait_ge(xn_ready, b + q + 1)
                if has(b, q, -1) or c >= 2:
                    pe.wait_ge(lo_ready, n - 1)
                for j in range(TPP):
                    last = nc.tensor.transpose(tp_ps[c % 2][:, j * P:(j + 1) * P], xn[:, j, c * P:(c + 1) * P], ident[:])
                last.then_inc(chunk_transposed, 1)

            def average(column, stat, done):
                nc.tensor.matmul(stat_ps[:, column:column + 1], averaging[:], stat, start=True, stop=True).then_inc(done, 1)

            def mean(b, q):
                pe.wait_ge(sum_ready, b + q + 1)
                if has(b, q, -1):
                    pe.wait_ge(var_eps_ready, b + q)
                average(0, sums[:, q % 2:q % 2 + 1], mean_ready)

            def variance(b, q):
                pe.wait_ge(squares_ready, b + q + 1)
                average(1, squares[:, q % 2:q % 2 + 1], var_ready)

            def lif_product(b, q, e):
                if e == 0:
                    pe.wait_ge(lo_ready, (b + q) * C + C)
                if has(b, q, -1) or e >= 2:
                    pe.wait_ge(u_ready, (b + q) * C + e - 1)
                hi, lo = xT[q % 2][:, 0], xT[q % 2][:, 1]
                cols = slice(e * P, (e + 1) * P)
                for k in range(C):
                    nc.tensor.matmul(y_ps[e % 2][:], wl[:, 1, k, cols], hi[:, k, :], start=k == 0, stop=False)
                    nc.tensor.matmul(y_ps[e % 2][:], wl[:, 0, k, cols], lo[:, k, :], start=False, stop=False)
                    last = nc.tensor.matmul(y_ps[e % 2][:], wl[:, 0, k, cols], hi[:, k, :], start=False, stop=k == C - 1)
                last.then_inc(y_ready, 1)

            def rec_product(b, q, j):
                if j == 0:
                    pe.wait_ge(gated_ready, (b + q) * C + C)
                if has(b, q, -1) or j >= 2:
                    pe.wait_ge(out_ready, (b + q) * TPP + j - 1)
                hi, lo = gated[q % 2][:, 0], gated[q % 2][:, 1]
                cols = slice(j * P, (j + 1) * P)
                for k in range(C):
                    nc.tensor.matmul(r_ps[j % 2][:], lo[:, k, cols], wr[:, 0, k, :], start=k == 0, stop=False)
                    nc.tensor.matmul(r_ps[j % 2][:], hi[:, k, cols], wr[:, 1, k, :], start=False, stop=False)
                    last = nc.tensor.matmul(r_ps[j % 2][:], hi[:, k, cols], wr[:, 0, k, :], start=False, stop=k == C - 1)
                last.then_inc(r_ready, 1)

            def transpose_mem(g):
                pe.wait_ge(mem_loaded[g], 16)
                for e in range(C):
                    if g or e:
                        pe.wait_ge(state_ready, g * C + e)
                    for j in range(TPP):
                        last = nc.tensor.transpose(mem_ps[:, j * P:(j + 1) * P],
                                                   x_ring[(4, 5, 7, 6)[g]][:, j, e * P:(e + 1) * P], ident[:])
                    last.then_inc(mem_transposed, 1)

            def step(b, q):
                for part in range(4):
                    if has(b, q, 1) and part < 2:
                        transpose_chunk(b, q + 1, 2 * part)
                        transpose_chunk(b, q + 1, 2 * part + 1)
                    if has(b, q, 0):
                        lif_product(b, q, part)
                    if has(b, q, 2) and part == 1:
                        mean(b, q + 2)
                    if has(b, q, 2) and part == 2:
                        variance(b, q + 2)
                    if has(b, q, -1):
                        rec_product(b, q - 1, part)

            pe.wait_ge(ident_ready, 1)
            pe.wait_ge(averaging_ready, 1)
            step(0, -2)
            transpose_mem(0)
            step(0, -1)
            transpose_mem(1)
            pe.wait_ge(wl_ready, 1)
            step(0, 0)
            transpose_mem(2)
            transpose_mem(3)
            pe.wait_ge(wr_ready, 1)
            for q in range(1, LOOP_FIRST):
                step(0, q)
            with pe.Fori(0, LOOP_END // SLOTS) as i:
                b = i * SLOTS
                for q in range(LOOP_FIRST, LOOP_FIRST + SLOTS):
                    step(b, q)
            for q in range(LOOP_FIRST, LAST_Q + 1):
                step(LOOP_END, q)


_INS = ["x", "L0_conv_tr_mx", "L0_conv_W_lif", "L0_conv_b_lif", "L0_conv_W_rec", "L0_conv_b_rec"]


def kernel(**inputs):
    import numpy as _np
    import concourse.bacc as _bacc
    from concourse import mybir as _mybir
    from concourse.bass_utils import run_bass_kernel_spmd as _run

    nc = _bacc.Bacc("TRN2", target_bir_lowering=False, num_devices=1)
    arrays, args = {}, []
    for name in _INS:
        a = _np.ascontiguousarray(inputs[name])
        arrays[f"in_{name}_dram"] = a
        args.append(nc.dram_tensor(f"in_{name}_dram", a.shape, _mybir.dt.from_np(a.dtype), kind="ExternalInput").ap())
    out_shape = arrays["in_x_dram"].shape
    args.append(nc.dram_tensor("out_0_dram", out_shape, _mybir.dt.float32, kind="ExternalOutput").ap())
    lif_block(nc, *args)
    r = _run(nc, [arrays], core_ids=[0])
    return r.results[0]["out_0_dram"]
```

```python
from contextlib import ExitStack

import concourse.bass as bass
from concourse import mybir

P = 128
QUAD = 32
BANK = 512


def lif_block(nc: bass.Bass, x, tr_mx, w_lif, b_lif, w_rec, b_rec, out):
    f32 = mybir.dt.float32
    f32r = mybir.dt.float32r
    bf16 = mybir.dt.bfloat16
    ALU = mybir.AluOpType
    ACT = mybir.ActivationFunctionType

    T, B, N, D = x.shape
    GROUPS = 4
    R = B // GROUPS * N
    TPP = R // P
    C = D // P
    Q = P // QUAD
    M = R // QUAD
    S = T * GROUPS
    EPS = 1e-5
    SLOTS = 4
    AHEAD_BLK = 4
    AHEAD_NAT = 2
    BLK_INC = 16 * Q
    assert R == BANK and D == BANK and TPP == C == Q == GROUPS == SLOTS == 4

    x_rows = x.rearrange("t b n d -> (t b n) d")
    x_blk = x_rows.rearrange("(s m i) (q f) -> s q i m f", m=M, i=QUAD, q=Q)
    x_nat = x_rows.rearrange("(s j p) d -> s p j d", p=P, j=TPP)
    out_nat = out.rearrange("t b n d -> (t b n) d").rearrange("(s j p) d -> s p j d", p=P, j=TPP)
    mem_blk = tr_mx.rearrange("b n d -> (b n) d").rearrange("(g m i) (q f) -> g q i m f", m=M, i=QUAD, q=Q)
    w_lif_rows = w_lif.rearrange("(q c i) e -> q i c e", q=Q, i=QUAD)
    w_rec_rows = w_rec.rearrange("(q c i) e -> q i c e", q=Q, i=QUAD)
    b_lif_rows = b_lif.rearrange("(q c i) -> q i c", q=Q, i=QUAD)

    with ExitStack() as ctx:
        def sb(name, shape, dt=f32):
            return ctx.enter_context(nc.sbuf_tensor(name, shape, dt))

        def pb(name):
            return ctx.enter_context(nc.psum_tensor(name, [P, BANK], f32))

        def sem(name):
            return ctx.enter_context(nc.semaphore(name))

        blk_ring = [sb(f"blk_ring{i}", [P, M, P]) for i in range(SLOTS)]
        nat_ring = [sb(f"nat_ring{i}", [P, TPP, D]) for i in range(SLOTS)]
        unused = sb("unused", [P, M * P], bf16)
        xT = [sb(f"xT{i}", [P, 2, C, R], f32r) for i in range(2)]
        gated = [sb(f"gated{i}", [P, 2, C, R], f32r) for i in range(2)]
        state = [sb(f"state{g}", [P, C, R]) for g in range(GROUPS)]
        u_buf = [sb(f"u{i}", [P, R]) for i in range(2)]
        wl = sb("wl", [P, 2, C, D], f32r)
        wr = sb("wr", [P, 2, C, D], f32r)
        b_rec_bc = sb("b_rec_bc", [P, D])
        b_lif_col = sb("b_lif_col", [P, C])
        averaging = sb("averaging", [P, P])
        minus_half = sb("minus_half", [P, 2])
        sums = sb("sums", [P, 2])
        squares = sb("squares", [P, 2])
        neg_mean = sb("neg_mean", [P, 2])
        var_eps = sb("var_eps", [P, 2])
        rstd = sb("rstd", [P, 2])
        shift = sb("shift", [P, 2])
        raw_w_lif, raw_w_rec = state[3], state[2]

        TB = 3
        xT_ps = [pb(f"xT_ps{i}") for i in range(TB)]
        y_ps = [pb(f"y_ps{i}") for i in range(2)]
        r_ps = [pb(f"r_ps{i}") for i in range(2)]
        stat_ps = pb("stat_ps")

        blk_loaded = [sem(f"blk_loaded{i}") for i in range(SLOTS)]
        nat_loaded = [sem(f"nat_loaded{i}") for i in range(SLOTS)]
        out_stored = [sem(f"out_stored{i}") for i in range(SLOTS)]
        w_lif_loaded = sem("w_lif_loaded")
        w_rec_loaded = sem("w_rec_loaded")
        b_lif_loaded = sem("b_lif_loaded")
        b_rec_loaded = sem("b_rec_loaded")
        mem_loaded = [sem(f"mem_loaded{g}") for g in range(GROUPS)]
        averaging_ready = sem("averaging_ready")
        half_ready = sem("half_ready")
        wl_hi_ready = sem("wl_hi_ready")
        wl_ready = sem("wl_ready")
        wr_hi_ready = sem("wr_hi_ready")
        wr_ready = sem("wr_ready")
        mem_transposed = sem("mem_transposed")
        sum_ready = sem("sum_ready")
        mean_ready = sem("mean_ready")
        neg_mean_ready = sem("neg_mean_ready")
        var_ready = sem("var_ready")
        var_eps_ready = sem("var_eps_ready")
        rstd_ready = sem("rstd_ready")
        shift_ready = sem("shift_ready")
        squares_ready = sem("squares_ready")
        xn_ready = sem("xn_ready")
        residual_ready = sem("residual_ready")
        chunk_transposed = sem("chunk_transposed")
        hi_ready = sem("hi_ready")
        lo_ready = sem("lo_ready")
        y_ready = sem("y_ready")
        u_ready = sem("u_ready")
        gated_ready = sem("gated_ready")
        reset_done = sem("reset_done")
        state_ready = sem("state_ready")
        r_ready = sem("r_ready")
        out_ready = sem("out_ready")

        block = ctx.enter_context(nc.Block())

        LOOP_FIRST = 4
        LOOPS = (S - AHEAD_BLK - LOOP_FIRST) // SLOTS
        LOOP_END = LOOPS * SLOTS
        LAST_Q = S - LOOP_END

        def has(b, q, d):
            return not isinstance(b, int) or 0 <= b + q + d < S

        def starts_pair(b, q):
            return q % 2 == 0 and has(b, q, 2)

        def dma_count(b, q, inc=16):
            return b * (inc // SLOTS) + inc * (q // SLOTS + 1)

        @block.sync
        def _(sp):
            def by_quadrant(dst, src, signal, inc=16):
                for h in range(Q):
                    sp.dma_start(dst[h * QUAD:(h + 1) * QUAD], src[h]).then_inc(signal, inc)

            def load_blk(b, q):
                for h in range(Q):
                    sp.dma_start(blk_ring[q % SLOTS][h * QUAD:(h + 1) * QUAD],
                                 x_blk[b + q, h]).then_inc(blk_loaded[q % SLOTS], 16)

            def load_nat(b, q):
                sp.dma_start(nat_ring[q % SLOTS][:], x_nat[b + q]).then_inc(nat_loaded[q % SLOTS], 16)

            def step(b, q):
                if has(b, q, AHEAD_BLK):
                    sp.wait_ge(chunk_transposed, (b + q) * C + C)
                    load_blk(b, q + AHEAD_BLK)
                if has(b, q, AHEAD_NAT):
                    if has(b, q, AHEAD_NAT - SLOTS):
                        sp.wait_ge(out_stored[(q + AHEAD_NAT) % SLOTS], dma_count(b, q + AHEAD_NAT - SLOTS))
                    else:
                        sp.wait_ge(mem_transposed, (b + q + AHEAD_NAT + 1) * C)
                    load_nat(b, q + AHEAD_NAT)
                if has(b, q, -1):
                    sp.wait_ge(out_ready, (b + q) * TPP)
                    sp.dma_start(out_nat[b + q - 1], nat_ring[(q - 1) % SLOTS][:]).then_inc(out_stored[(q - 1) % SLOTS], 16)

            load_blk(0, 0)
            load_blk(0, 1)
            for h in range(Q):
                sp.dma_start(raw_w_lif[h * QUAD:(h + 1) * QUAD], w_lif_rows[h]).then_inc(w_lif_loaded, 16)
            for h in range(Q):
                sp.dma_start(b_lif_col[h * QUAD:(h + 1) * QUAD], b_lif_rows[h],
                             allow_slow_non_contiguous=True).then_inc(b_lif_loaded, 16)
            for g in range(GROUPS):
                for h in range(Q):
                    sp.dma_start(nat_ring[g][h * QUAD:(h + 1) * QUAD].rearrange("p j d -> p (j d)").rearrange("p (m f) -> p m f", m=M),
                                 mem_blk[g, h]).then_inc(mem_loaded[g], 16)
                if g == 0:
                    sp.dma_start(b_rec_bc[:], b_rec.partition_broadcast(P)).then_inc(b_rec_loaded, 16)
                    for h in range(Q):
                        sp.dma_start(raw_w_rec[h * QUAD:(h + 1) * QUAD], w_rec_rows[h]).then_inc(w_rec_loaded, 16)
                    load_blk(0, 2)
                    load_blk(0, 3)
            for q in range(-AHEAD_NAT, 0):
                sp.wait_ge(mem_transposed, (q + AHEAD_NAT + 1) * C)
                load_nat(0, q + AHEAD_NAT)
            for q in range(LOOP_FIRST):
                step(0, q)
            with sp.Fori(0, LOOPS) as i:
                for q in range(LOOP_FIRST, LOOP_FIRST + SLOTS):
                    step(i * SLOTS, q)
            for q in range(LOOP_FIRST, LAST_Q + 1):
                step(LOOP_END, q)
            for i in range(SLOTS):
                sp.wait_ge(out_stored[i], 16 * (S // SLOTS))

        @block.gpsimd
        def _(pool):
            nc.gpsimd.memset(averaging[:], 1.0 / (R * D)).then_inc(averaging_ready, 1)
            nc.gpsimd.memset(minus_half[:], -0.5).then_inc(half_ready, 1)
            pool.wait_ge(half_ready, 1)

            def step(b, q):
                if starts_pair(b, q):
                    n = b + q + 4
                    pool.wait_ge(var_eps_ready, n)
                    nc.gpsimd.tensor_tensor(rstd[:], var_eps[:], minus_half[:], ALU.pow).then_inc(rstd_ready, 2)
                    pool.wait_ge(rstd_ready, n)
                    nc.gpsimd.tensor_tensor(shift[:], neg_mean[:], rstd[:], ALU.mult).then_inc(shift_ready, 2)
                if has(b, q, 1):
                    slot = nat_ring[(q + 1) % SLOTS]
                    pool.wait_ge(nat_loaded[(q + 1) % SLOTS], dma_count(b, q + 1))
                    nc.gpsimd.tensor_tensor(slot[:], slot[:], b_rec_bc[:].unsqueeze(1).broadcast_to([P, TPP, D]),
                                            ALU.add).then_inc(residual_ready, 1)

            step(0, -2)
            pool.wait_ge(b_rec_loaded, 16)
            for q in range(-1, LOOP_FIRST):
                step(0, q)
            with pool.Fori(0, LOOPS) as i:
                for q in range(LOOP_FIRST, LOOP_FIRST + SLOTS):
                    step(i * SLOTS, q)
            for q in range(LOOP_FIRST, LAST_Q + 1):
                step(LOOP_END, q)

        @block.scalar
        def _(act):
            def hi_part(b, q, c):
                act.wait_ge(chunk_transposed, (b + q) * C + c + 1)
                nc.scalar.activation(xT[q % 2][:, 0, c, :], xT_ps[c % TB][:], ACT.Copy).then_inc(hi_ready, 1)

            def total(b, q):
                act.wait_ge(blk_loaded[q % SLOTS], dma_count(b, q, BLK_INC))
                if has(b, q, -1):
                    act.wait_ge(sum_ready if q % 2 else squares_ready, b + q)
                nc.scalar.activation(unused[:], blk_ring[q % SLOTS][:].rearrange("p m f -> p (m f)"), ACT.Copy,
                                     accum_out=sums[:, q % 2:q % 2 + 1]).then_inc(sum_ready, 1)

            def negate_means(b, q):
                act.wait_ge(mean_ready, b + q + 2)
                nc.scalar.activation(neg_mean[:], stat_ps[:, 0:2], ACT.Copy, scale=-1.0).then_inc(neg_mean_ready, 2)
                act.wait_ge(neg_mean_ready, b + q + 2)

            def deviations(b, q):
                if q % 2:
                    act.wait_ge(squares_ready, b + q)
                nc.scalar.activation(unused[:], blk_ring[q % SLOTS][:].rearrange("p m f -> p (m f)"), ACT.Square,
                                     bias=neg_mean[:, q % 2:q % 2 + 1],
                                     accum_out=squares[:, q % 2:q % 2 + 1]).then_inc(squares_ready, 1)

            def normalise(b, q):
                act.wait_ge(shift_ready, b + q - q % 2 + 2)
                slot = blk_ring[q % SLOTS]
                nc.scalar.activation(slot[:], slot[:], ACT.Identity, bias=shift[:, q % 2:q % 2 + 1],
                                     scale=rstd[:, q % 2:q % 2 + 1]).then_inc(xn_ready, 1)

            def halve(b, q, e):
                act.wait_ge(reset_done, (b + q) * C + e + 1)
                st = state[q % GROUPS][:, e, :]
                nc.scalar.activation(st, st, ACT.Identity, bias=b_lif_col[:, e:e + 1], scale=0.5).then_inc(state_ready, 1)

            def first_state(g):
                for e in range(C):
                    act.wait_ge(mem_transposed, g * C + e + 1)
                    st = state[g][:, e, :]
                    nc.scalar.activation(st, st, ACT.Identity, bias=b_lif_col[:, e:e + 1]).then_inc(state_ready, 1)

            def step(b, q):
                if starts_pair(b, q):
                    total(b, q + 2)
                    total(b, q + 3)
                if has(b, q, 1):
                    if has(b, q, -1):
                        act.wait_ge(gated_ready, (b + q) * C)
                    hi_part(b, q + 1, 0)
                    hi_part(b, q + 1, 1)
                if starts_pair(b, q):
                    negate_means(b, q + 2)
                    deviations(b, q + 2)
                if has(b, q, 1):
                    hi_part(b, q + 1, 2)
                    hi_part(b, q + 1, 3)
                if starts_pair(b, q):
                    deviations(b, q + 3)
                if has(b, q, -1):
                    for e in range(C):
                        halve(b, q - 1, e)
                if has(b, q, 2):
                    normalise(b, q + 2)

            step(0, -2)
            act.wait_ge(b_lif_loaded, 16 * Q)
            first_state(0)
            step(0, -1)
            first_state(1)
            step(0, 0)
            first_state(2)
            first_state(3)
            for q in range(1, LOOP_FIRST):
                step(0, q)
            with act.Fori(0, LOOPS) as i:
                for q in range(LOOP_FIRST, LOOP_FIRST + SLOTS):
                    step(i * SLOTS, q)
            for q in range(LOOP_FIRST, LAST_Q + 1):
                step(LOOP_END, q)

        @block.vector
        def _(dve):
            def split_weight(raw, parts, ordered, loaded, hi_sem, both_sem):
                dve.wait_ge(loaded, 16 * Q)
                for k in range(C):
                    hi, lo = ordered(parts[:, 0, k, :], False), ordered(parts[:, 1, k, :], False)
                    nc.vector.tensor_copy(hi, ordered(raw[:, k, :], True)).then_inc(hi_sem, 1)
                    dve.wait_ge(hi_sem, k + 1)
                    nc.vector.tensor_tensor(lo, ordered(raw[:, k, :], True), hi.bitcast(f32), ALU.subtract).then_inc(both_sem, 1)

            def by_feature_chunk(ap, raw):
                order = "p (q c i) -> p q c i" if raw else "p (c q i) -> p q c i"
                return ap.rearrange(order, q=Q, i=QUAD)

            def as_they_are(ap, raw):
                return ap

            def transpose_chunk(b, q, c):
                if c == 0:
                    dve.wait_ge(xn_ready, b + q + 1)
                if c == TB:
                    dve.wait_ge(lo_ready, (b + q) * C + 1)
                elif has(b, q, -1) and c == 0:
                    dve.wait_ge(lo_ready, (b + q) * C)
                nc.vector.transpose(xT_ps[c % TB][:], blk_ring[q % SLOTS][:, :, c * QUAD:(c + 1) * QUAD]
                                    ).then_inc(chunk_transposed, 1)

            def transpose_mem(g):
                dve.wait_ge(mem_loaded[g], 16 * Q)
                blocked = nat_ring[g][:].rearrange("p j d -> p (j d)").rearrange("p (m f) -> p m f", m=M)
                for c in range(C):
                    nc.vector.transpose(state[g][:, c, :], blocked[:, :, c * QUAD:(c + 1) * QUAD]).then_inc(mem_transposed, 1)

            def lo_part(b, q, c):
                dve.wait_ge(hi_ready, (b + q) * C + c + 1)
                nc.vector.tensor_tensor(xT[q % 2][:, 1, c, :], xT_ps[c % TB][:], xT[q % 2][:, 0, c, :].bitcast(f32),
                                        ALU.subtract).then_inc(lo_ready, 1)

            def spike(b, q, e):
                n = (b + q) * C + e + 1
                u, st = u_buf[e % 2], state[q % GROUPS][:, e, :]
                dve.wait_ge(y_ready, n)
                dve.wait_ge(state_ready, n)
                nc.vector.tensor_tensor(u[:], y_ps[e % 2][:], st, ALU.add).then_inc(u_ready, 1)
                dve.wait_ge(u_ready, n)
                nc.vector.scalar_tensor_tensor(gated[q % 2][:, :, e, :], u[:].unsqueeze(1).broadcast_to([P, 2, R]), 2.0,
                                               xT[q % 2][:, :, e, :].bitcast(f32), ALU.is_le, ALU.mult).then_inc(gated_ready, 1)
                nc.vector.scalar_tensor_tensor(st, u[:], 2.0, u[:], ALU.is_le, ALU.mult).then_inc(reset_done, 1)

            def output(b, q, j):
                dve.wait_ge(r_ready, (b + q) * TPP + j + 1)
                if j == 0:
                    dve.wait_ge(residual_ready, b + q + 1)
                rows = nat_ring[q % SLOTS][:, j, :]
                nc.vector.tensor_tensor(rows, r_ps[j % 2][:], rows, ALU.add).then_inc(out_ready, 1)

            def add_eps(b, q):
                dve.wait_ge(var_ready, b + q + 2)
                nc.vector.tensor_scalar(var_eps[:], stat_ps[:, 2:4], EPS, None, ALU.add).then_inc(var_eps_ready, 2)

            def step(b, q):
                if has(b, q, 1):
                    transpose_chunk(b, q + 1, 0)
                    transpose_chunk(b, q + 1, 1)
                for part in range(4):
                    if has(b, q, 0):
                        spike(b, q, part)
                    if has(b, q, 1):
                        if part == 0:
                            lo_part(b, q + 1, 0)
                            transpose_chunk(b, q + 1, 2)
                            lo_part(b, q + 1, 1)
                            transpose_chunk(b, q + 1, 3)
                        if part == 1:
                            lo_part(b, q + 1, 2)
                            lo_part(b, q + 1, 3)
                    if has(b, q, -1):
                        output(b, q - 1, part)
                    if starts_pair(b, q) and part == 2:
                        add_eps(b, q + 2)

            split_weight(raw_w_lif, wl, by_feature_chunk, w_lif_loaded, wl_hi_ready, wl_ready)
            transpose_mem(0)
            step(0, -2)
            split_weight(raw_w_rec, wr, as_they_are, w_rec_loaded, wr_hi_ready, wr_ready)
            step(0, -1)
            transpose_mem(1)
            step(0, 0)
            transpose_mem(2)
            transpose_mem(3)
            for q in range(1, LOOP_FIRST):
                step(0, q)
            with dve.Fori(0, LOOPS) as i:
                for q in range(LOOP_FIRST, LOOP_FIRST + SLOTS):
                    step(i * SLOTS, q)
            for q in range(LOOP_FIRST, LAST_Q + 1):
                step(LOOP_END, q)

        @block.tensor
        def _(pe):
            def means(b, q):
                pe.wait_ge(sum_ready, b + q + 2)
                if has(b, q, -2):
                    pe.wait_ge(var_eps_ready, b + q)
                nc.tensor.matmul(stat_ps[:, 0:2], averaging[:], sums[:], start=True, stop=True).then_inc(mean_ready, 2)

            def variances(b, q):
                pe.wait_ge(squares_ready, b + q + 2)
                nc.tensor.matmul(stat_ps[:, 2:4], averaging[:], squares[:], start=True, stop=True).then_inc(var_ready, 2)

            def lif_product(b, q, e):
                if e == 0:
                    pe.wait_ge(lo_ready, (b + q) * C + C)
                if has(b, q, -1) or e >= 2:
                    pe.wait_ge(u_ready, (b + q) * C + e - 1)
                hi, lo = xT[q % 2][:, 0], xT[q % 2][:, 1]
                cols = slice(e * P, (e + 1) * P)
                for k in range(C):
                    nc.tensor.matmul(y_ps[e % 2][:], wl[:, 1, k, cols], hi[:, k, :], start=k == 0, stop=False)
                    nc.tensor.matmul(y_ps[e % 2][:], wl[:, 0, k, cols], lo[:, k, :], start=False, stop=False)
                    last = nc.tensor.matmul(y_ps[e % 2][:], wl[:, 0, k, cols], hi[:, k, :], start=False, stop=k == C - 1)
                last.then_inc(y_ready, 1)

            def rec_product(b, q, j):
                if j == 0:
                    pe.wait_ge(gated_ready, (b + q) * C + C)
                if has(b, q, -1) or j >= 2:
                    pe.wait_ge(out_ready, (b + q) * TPP + j - 1)
                hi, lo = gated[q % 2][:, 0], gated[q % 2][:, 1]
                cols = slice(j * P, (j + 1) * P)
                for k in range(C):
                    nc.tensor.matmul(r_ps[j % 2][:], lo[:, k, cols], wr[:, 0, k, :], start=k == 0, stop=False)
                    nc.tensor.matmul(r_ps[j % 2][:], hi[:, k, cols], wr[:, 1, k, :], start=False, stop=False)
                    last = nc.tensor.matmul(r_ps[j % 2][:], hi[:, k, cols], wr[:, 0, k, :], start=False, stop=k == C - 1)
                last.then_inc(r_ready, 1)

            def step(b, q):
                for part in range(4):
                    if has(b, q, 0):
                        lif_product(b, q, part)
                    if has(b, q, -1):
                        rec_product(b, q - 1, part)
                    if starts_pair(b, q) and part == 0:
                        means(b, q + 2)
                    if starts_pair(b, q) and part == 2:
                        variances(b, q + 2)

            pe.wait_ge(averaging_ready, 1)
            step(0, -2)
            pe.wait_ge(wl_ready, C)
            step(0, -1)
            step(0, 0)
            pe.wait_ge(wr_ready, C)
            for q in range(1, LOOP_FIRST):
                step(0, q)
            with pe.Fori(0, LOOPS) as i:
                for q in range(LOOP_FIRST, LOOP_FIRST + SLOTS):
                    step(i * SLOTS, q)
            for q in range(LOOP_FIRST, LAST_Q + 1):
                step(LOOP_END, q)


_INS = ["x", "L0_conv_tr_mx", "L0_conv_W_lif", "L0_conv_b_lif", "L0_conv_W_rec", "L0_conv_b_rec"]


def kernel(**inputs):
    import numpy as _np
    import concourse.bacc as _bacc
    from concourse import mybir as _mybir
    from concourse.bass_utils import run_bass_kernel_spmd as _run

    nc = _bacc.Bacc("TRN2", target_bir_lowering=False, num_devices=1)
    arrays, args = {}, []
    for name in _INS:
        a = _np.ascontiguousarray(inputs[name])
        arrays[f"in_{name}_dram"] = a
        args.append(nc.dram_tensor(f"in_{name}_dram", a.shape, _mybir.dt.from_np(a.dtype), kind="ExternalInput").ap())
    out_shape = arrays["in_x_dram"].shape
    args.append(nc.dram_tensor("out_0_dram", out_shape, _mybir.dt.float32, kind="ExternalOutput").ap())
    lif_block(nc, *args)
    r = _run(nc, [arrays], core_ids=[0])
    return r.results[0]["out_0_dram"]
```

```python
from contextlib import ExitStack

import concourse.bass as bass
from concourse import mybir

P = 128
QUAD = 32
BANK = 512


def lif_block(nc: bass.Bass, x, tr_mx, w_lif, b_lif, w_rec, b_rec, out):
    f32 = mybir.dt.float32
    f32r = mybir.dt.float32r
    bf16 = mybir.dt.bfloat16
    ALU = mybir.AluOpType
    ACT = mybir.ActivationFunctionType

    T, B, N, D = x.shape
    GROUPS = 4
    R = B // GROUPS * N
    TPP = R // P
    C = D // P
    Q = P // QUAD
    M = R // QUAD
    S = T * GROUPS
    EPS = 1e-5
    SLOTS = 4
    AHEAD_BLK = 4
    AHEAD_NAT = 2
    BLK_INC = 16 * Q
    assert R == BANK and D == BANK and TPP == C == Q == GROUPS == SLOTS == 4

    x_rows = x.rearrange("t b n d -> (t b n) d")
    x_blk = x_rows.rearrange("(s m i) (q f) -> s q i m f", m=M, i=QUAD, q=Q)
    x_nat = x_rows.rearrange("(s j p) d -> s p j d", p=P, j=TPP)
    out_nat = out.rearrange("t b n d -> (t b n) d").rearrange("(s j p) d -> s p j d", p=P, j=TPP)
    mem_blk = tr_mx.rearrange("b n d -> (b n) d").rearrange("(g m i) (q f) -> g q i m f", m=M, i=QUAD, q=Q)
    w_lif_rows = w_lif.rearrange("(q c i) e -> q i c e", q=Q, i=QUAD)
    w_rec_rows = w_rec.rearrange("(q c i) e -> q i c e", q=Q, i=QUAD)
    b_lif_rows = b_lif.rearrange("(q c i) -> q i c", q=Q, i=QUAD)

    with ExitStack() as ctx:
        def sb(name, shape, dt=f32):
            return ctx.enter_context(nc.sbuf_tensor(name, shape, dt))

        def pb(name, shape=(P, BANK)):
            return ctx.enter_context(nc.psum_tensor(name, list(shape), f32))

        def sem(name):
            return ctx.enter_context(nc.semaphore(name))

        blk_ring = [sb(f"blk_ring{i}", [P, M, P]) for i in range(SLOTS)]
        nat_ring = [sb(f"nat_ring{i}", [P, TPP, D]) for i in range(SLOTS)]
        unused = sb("unused", [P, M * P], bf16)
        xT = [sb(f"xT{i}", [P, 2, C, R], f32r) for i in range(2)]
        gated = [sb(f"gated{i}", [P, 2, C, R], f32r) for i in range(2)]
        state = [sb(f"state{g}", [P, C, R]) for g in range(GROUPS)]
        u_buf = sb("u", [P, 2, R])
        wl = sb("wl", [P, 2, C, D], f32r)
        wr = sb("wr", [P, 2, C, D], f32r)
        b_rec_bc = sb("b_rec_bc", [P, D])
        b_lif_col = sb("b_lif_col", [P, C])
        averaging = sb("averaging", [P, P])
        minus_half = sb("minus_half", [P, 2])
        sums = sb("sums", [P, 2])
        squares = sb("squares", [P, 2])
        neg_mean = sb("neg_mean", [P, 2])
        var_eps = sb("var_eps", [P, 2])
        rstd = sb("rstd", [P, 2])
        shift = sb("shift", [P, 2])
        raw_w_lif, raw_w_rec = state[3], state[2]

        xT_ps = pb("xT_ps", (P, 2, BANK))
        y_ps = [pb(f"y_ps{i}") for i in range(2)]
        r_ps = pb("r_ps", (P, 2, BANK))
        stat_ps = pb("stat_ps")

        blk_loaded = [sem(f"blk_loaded{i}") for i in range(SLOTS)]
        nat_loaded = [sem(f"nat_loaded{i}") for i in range(SLOTS)]
        out_stored = [sem(f"out_stored{i}") for i in range(SLOTS)]
        w_lif_loaded = sem("w_lif_loaded")
        w_rec_loaded = sem("w_rec_loaded")
        b_lif_loaded = sem("b_lif_loaded")
        b_rec_loaded = sem("b_rec_loaded")
        mem_loaded = [sem(f"mem_loaded{g}") for g in range(GROUPS)]
        averaging_ready = sem("averaging_ready")
        half_ready = sem("half_ready")
        wl_hi_ready = sem("wl_hi_ready")
        wl_ready = sem("wl_ready")
        wr_hi_ready = sem("wr_hi_ready")
        wr_ready = sem("wr_ready")
        mem_transposed = sem("mem_transposed")
        sum_ready = sem("sum_ready")
        mean_ready = sem("mean_ready")
        neg_mean_ready = sem("neg_mean_ready")
        var_ready = sem("var_ready")
        var_eps_ready = sem("var_eps_ready")
        rstd_ready = sem("rstd_ready")
        shift_ready = sem("shift_ready")
        squares_ready = sem("squares_ready")
        xn_ready = sem("xn_ready")
        chunk_transposed = sem("chunk_transposed")
        hi_ready = sem("hi_ready")
        lo_ready = sem("lo_ready")
        y_ready = sem("y_ready")
        u_ready = sem("u_ready")
        gated_ready = sem("gated_ready")
        reset_done = sem("reset_done")
        state_ready = sem("state_ready")
        residual_ready = sem("residual_ready")
        r_ready = sem("r_ready")
        out_ready = sem("out_ready")

        block = ctx.enter_context(nc.Block())

        LOOP_FIRST = 4
        LOOPS = (S - AHEAD_BLK - LOOP_FIRST) // SLOTS
        LOOP_END = LOOPS * SLOTS
        LAST_Q = S - LOOP_END

        def has(b, q, d):
            return not isinstance(b, int) or 0 <= b + q + d < S

        def starts_pair(b, q):
            return q % 2 == 0 and has(b, q, 2)

        def variances_after(b, q):
            if isinstance(b, int) and b + q < 2:
                return 0 if b + q == 1 else None
            return 3 if starts_pair(b, q) else None

        def is_early(b, q):
            return isinstance(b, int) and b + q < 2

        def transposed_ps(b, q, c):
            return r_ps if is_early(b, q) and c else xT_ps

        def dma_count(b, q, inc=16):
            return b * (inc // SLOTS) + inc * (q // SLOTS + 1)

        @block.sync
        def _(sp):
            def load_blk(b, q):
                for h in range(Q):
                    sp.dma_start(blk_ring[q % SLOTS][h * QUAD:(h + 1) * QUAD],
                                 x_blk[b + q, h]).then_inc(blk_loaded[q % SLOTS], 16)

            def load_nat(b, q):
                sp.dma_start(nat_ring[q % SLOTS][:], x_nat[b + q]).then_inc(nat_loaded[q % SLOTS], 16)

            def replace_blk(b, q):
                sp.wait_ge(chunk_transposed, (b + q - AHEAD_BLK) * C + C)
                load_blk(b, q)

            def first_nat(q):
                sp.wait_ge(mem_transposed, (q + 1) * C)
                load_nat(0, q)

            def store(b, q):
                sp.wait_ge(out_ready, (b + q + 1) * TPP)
                sp.dma_start(out_nat[b + q], nat_ring[q % SLOTS][:]).then_inc(out_stored[q % SLOTS], 16)

            def step(b, q):
                if has(b, q, AHEAD_BLK):
                    replace_blk(b, q + AHEAD_BLK)
                if has(b, q, AHEAD_NAT):
                    sp.wait_ge(out_stored[(q + AHEAD_NAT) % SLOTS], dma_count(b, q + AHEAD_NAT - SLOTS))
                    load_nat(b, q + AHEAD_NAT)
                store(b, q - 1)

            load_blk(0, 0)
            for h in range(Q):
                sp.dma_start(raw_w_lif[h * QUAD:(h + 1) * QUAD], w_lif_rows[h]).then_inc(w_lif_loaded, 16)
            load_blk(0, 1)
            for h in range(Q):
                sp.dma_start(b_lif_col[h * QUAD:(h + 1) * QUAD], b_lif_rows[h],
                             allow_slow_non_contiguous=True).then_inc(b_lif_loaded, 16)
            for g in range(GROUPS):
                for h in range(Q):
                    sp.dma_start(nat_ring[g][h * QUAD:(h + 1) * QUAD].rearrange("p j d -> p (j d)").rearrange("p (m f) -> p m f", m=M),
                                 mem_blk[g, h]).then_inc(mem_loaded[g], 16)
                if g == 0:
                    sp.dma_start(b_rec_bc[:], b_rec.partition_broadcast(P)).then_inc(b_rec_loaded, 16)
                    for h in range(Q):
                        sp.dma_start(raw_w_rec[h * QUAD:(h + 1) * QUAD], w_rec_rows[h]).then_inc(w_rec_loaded, 16)
                    load_blk(0, 2)
                    load_blk(0, 3)
            first_nat(0)
            first_nat(1)
            replace_blk(0, 4)
            replace_blk(0, 5)
            first_nat(2)
            store(0, 0)
            step(0, 2)
            first_nat(3)
            step(0, 3)
            with sp.Fori(0, LOOPS) as i:
                for q in range(LOOP_FIRST, LOOP_FIRST + SLOTS):
                    step(i * SLOTS, q)
            for q in range(LOOP_FIRST, LAST_Q + 1):
                step(LOOP_END, q)
            for i in range(SLOTS):
                sp.wait_ge(out_stored[i], 16 * (S // SLOTS))

        @block.gpsimd
        def _(pool):
            nc.gpsimd.memset(averaging[:], 1.0 / (R * D)).then_inc(averaging_ready, 1)
            nc.gpsimd.memset(minus_half[:], -0.5).then_inc(half_ready, 1)
            pool.wait_ge(half_ready, 1)

            def scales(b, q, n=2):
                cols = slice(q % 2, q % 2 + n)
                pool.wait_ge(var_eps_ready, b + q + n)
                nc.gpsimd.tensor_tensor(rstd[:, cols], var_eps[:, cols], minus_half[:, cols], ALU.pow).then_inc(rstd_ready, n)
                pool.wait_ge(rstd_ready, b + q + n)
                nc.gpsimd.tensor_tensor(shift[:, cols], neg_mean[:, cols], rstd[:, cols], ALU.mult).then_inc(shift_ready, n)

            def add_bias(b, q, j):
                if j == 0:
                    pool.wait_ge(nat_loaded[q % SLOTS], dma_count(b, q))
                rows = nat_ring[q % SLOTS][:, j, :]
                nc.gpsimd.tensor_tensor(rows, rows, b_rec_bc[:], ALU.add).then_inc(residual_ready, 1)

            def step(b, q):
                if starts_pair(b, q):
                    scales(b, q + 2)
                if has(b, q, 1):
                    for j in range(TPP):
                        add_bias(b, q + 1, j)

            for q in range(2):
                scales(0, q, 1)
            for k in range(C):
                pool.wait_ge(wr_hi_ready, k + 1)
                nc.gpsimd.tensor_tensor(wr[:, 1, k, :], raw_w_rec[:, k, :], wr[:, 0, k, :].bitcast(f32),
                                        ALU.subtract).then_inc(wr_ready, 1)
            pool.wait_ge(b_rec_loaded, 16)
            for j in range(TPP):
                add_bias(0, 0, j)
            for q in range(LOOP_FIRST):
                step(0, q)
            with pool.Fori(0, LOOPS) as i:
                for q in range(LOOP_FIRST, LOOP_FIRST + SLOTS):
                    step(i * SLOTS, q)
            for q in range(LOOP_FIRST, LAST_Q + 1):
                step(LOOP_END, q)

        @block.scalar
        def _(act):
            def hi_part(b, q, c):
                act.wait_ge(chunk_transposed, (b + q) * C + c + 2)
                nc.scalar.activation(xT[q % 2][:, 0, c:c + 2, :], transposed_ps(b, q, c)[:], ACT.Copy).then_inc(hi_ready, 2)

            def total(b, q, n=2):
                act.wait_ge(blk_loaded[q % SLOTS], dma_count(b, q, BLK_INC))
                if has(b, q, -1):
                    act.wait_ge(sum_ready if q % 2 and n == 2 else squares_ready, b + q)
                nc.scalar.activation(unused[:], blk_ring[q % SLOTS][:].rearrange("p m f -> p (m f)"), ACT.Copy,
                                     accum_out=sums[:, q % 2:q % 2 + 1]).then_inc(sum_ready, 1)

            def negate_means(b, q, n=2):
                cols = slice(q % 2, q % 2 + n)
                act.wait_ge(mean_ready, b + q + n)
                nc.scalar.activation(neg_mean[:, cols], stat_ps[:, cols], ACT.Copy, scale=-1.0).then_inc(neg_mean_ready, n)

            def deviations(b, q, n=2):
                if n == 1 or q % 2 == 0:
                    act.wait_ge(neg_mean_ready, b + q + n)
                else:
                    act.wait_ge(squares_ready, b + q)
                nc.scalar.activation(unused[:], blk_ring[q % SLOTS][:].rearrange("p m f -> p (m f)"), ACT.Square,
                                     bias=neg_mean[:, q % 2:q % 2 + 1],
                                     accum_out=squares[:, q % 2:q % 2 + 1]).then_inc(squares_ready, 1)

            def normalise(b, q, n=2):
                act.wait_ge(shift_ready, b + q + 1 if n == 1 else b + q - q % 2 + 2)
                slot = blk_ring[q % SLOTS]
                nc.scalar.activation(slot[:], slot[:], ACT.Identity, bias=shift[:, q % 2:q % 2 + 1],
                                     scale=rstd[:, q % 2:q % 2 + 1]).then_inc(xn_ready, 1)

            def halve(b, q, e):
                act.wait_ge(reset_done, (b + q) * C + e + 1)
                st = state[q % GROUPS][:, e, :]
                nc.scalar.activation(st, st, ACT.Identity, bias=b_lif_col[:, e:e + 1], scale=0.5).then_inc(state_ready, 1)

            def first_state(g):
                for e in range(C):
                    act.wait_ge(mem_transposed, g * C + e + 1)
                    st = state[g][:, e, :]
                    nc.scalar.activation(st, st, ACT.Identity, bias=b_lif_col[:, e:e + 1]).then_inc(state_ready, 1)

            def halves(b, q):
                for e in range(C):
                    halve(b, q, e)

            def step(b, q, after_first_states=True):
                if starts_pair(b, q):
                    total(b, q + 2)
                    total(b, q + 3)
                if has(b, q, 1):
                    if has(b, q, -1):
                        act.wait_ge(gated_ready, (b + q) * C)
                    hi_part(b, q + 1, 0)
                if starts_pair(b, q):
                    negate_means(b, q + 2)
                    deviations(b, q + 2)
                if has(b, q, 1):
                    hi_part(b, q + 1, 2)
                if starts_pair(b, q):
                    deviations(b, q + 3)
                if after_first_states:
                    halves(b, q - 1)
                else:
                    first_state(q + 1)
                if has(b, q, 2):
                    normalise(b, q + 2)

            total(0, 0, 1)
            negate_means(0, 0, 1)
            deviations(0, 0, 1)
            normalise(0, 0, 1)
            total(0, 1, 1)
            negate_means(0, 1, 1)
            deviations(0, 1, 1)
            hi_part(0, 0, 0)
            hi_part(0, 0, 2)
            normalise(0, 1, 1)
            act.wait_ge(b_lif_loaded, 16 * Q)
            first_state(0)
            for q in range(GROUPS - 1):
                step(0, q, after_first_states=False)
            for q in range(GROUPS - 2):
                halves(0, q)
            step(0, GROUPS - 1)
            with act.Fori(0, LOOPS) as i:
                for q in range(LOOP_FIRST, LOOP_FIRST + SLOTS):
                    step(i * SLOTS, q)
            for q in range(LOOP_FIRST, LAST_Q + 1):
                step(LOOP_END, q)

        @block.vector
        def _(dve):
            def split_w_lif(chunks):
                dve.wait_ge(w_lif_loaded, 16 * Q)
                for k in chunks:
                    raw = raw_w_lif[:, k, :].rearrange("p (q c i) -> p q c i", q=Q, i=QUAD)
                    hi, lo = (wl[:, part, k, :].rearrange("p (c q i) -> p q c i", q=Q, i=QUAD) for part in range(2))
                    nc.vector.tensor_copy(hi, raw).then_inc(wl_hi_ready, 1)
                    dve.wait_ge(wl_hi_ready, k + 1)
                    nc.vector.tensor_tensor(lo, raw, hi.bitcast(f32), ALU.subtract).then_inc(wl_ready, 1)

            def transpose_chunks(b, q, c):
                if c == 0:
                    dve.wait_ge(xn_ready, b + q + 1)
                if has(b, q, -1) and transposed_ps(b, q, c) is xT_ps:
                    dve.wait_ge(lo_ready, (b + q) * C + c)
                chunks = blk_ring[q % SLOTS][:, :, c * QUAD:(c + 2) * QUAD].rearrange("p m (c i) -> p c m i", c=2)
                nc.vector.transpose(transposed_ps(b, q, c)[:].rearrange("p c (m i) -> p c m i", i=QUAD), chunks).then_inc(chunk_transposed, 2)

            def transpose_mem(g):
                dve.wait_ge(mem_loaded[g], 16 * Q)
                if g == 2:
                    dve.wait_ge(wr_ready, C)
                if g == 3:
                    dve.wait_ge(wl_ready, C)
                blocked = nat_ring[g][:].rearrange("p j d -> p (j d)").rearrange("p (m f) -> p m f", m=M)
                for c in range(C):
                    nc.vector.transpose(state[g][:, c, :], blocked[:, :, c * QUAD:(c + 1) * QUAD]).then_inc(mem_transposed, 1)

            def lo_part(b, q, c):
                dve.wait_ge(hi_ready, (b + q) * C + c + 2)
                nc.vector.tensor_tensor(xT[q % 2][:, 1, c:c + 2, :], transposed_ps(b, q, c)[:], xT[q % 2][:, 0, c:c + 2, :].bitcast(f32),
                                        ALU.subtract).then_inc(lo_ready, 2)

            def spike(b, q, e):
                n = (b + q) * C + e + 1
                u, st = u_buf[:, e % 2, :], state[q % GROUPS]
                dve.wait_ge(y_ready, n)
                dve.wait_ge(state_ready, n)
                if e % 2 == 0 and (has(b, q, -1) or e):
                    dve.wait_ge(reset_done, n - 1)
                nc.vector.tensor_tensor(u, y_ps[e % 2][:], st[:, e, :], ALU.add).then_inc(u_ready, 1)
                dve.wait_ge(u_ready, n)
                nc.vector.scalar_tensor_tensor(gated[q % 2][:, :, e, :], u.unsqueeze(1).broadcast_to([P, 2, R]), 2.0,
                                               xT[q % 2][:, :, e, :].bitcast(f32), ALU.is_le, ALU.mult).then_inc(gated_ready, 1)
                if e % 2:
                    nc.vector.scalar_tensor_tensor(st[:, e - 1:e + 1, :], u_buf[:], 2.0, u_buf[:],
                                                   ALU.is_le, ALU.mult).then_inc(reset_done, 2)

            def output(b, q, j):
                dve.wait_ge(r_ready, (b + q) * TPP + j + 1)
                dve.wait_ge(residual_ready, (b + q) * TPP + j + 1)
                rows = nat_ring[q % SLOTS][:, j, :]
                nc.vector.tensor_tensor(rows, r_ps[:, j % 2, :], rows, ALU.add).then_inc(out_ready, 1)

            def add_eps(b, q, n=2):
                dve.wait_ge(var_ready, b + q + n)
                nc.vector.tensor_scalar(var_eps[:, q % 2:q % 2 + n], stat_ps[:, 2 + q % 2:2 + q % 2 + n], EPS, None,
                                        ALU.add).then_inc(var_eps_ready, n)

            def step(b, q):
                for part in range(4):
                    if has(b, q, 0):
                        spike(b, q, part)
                    if has(b, q, 1) and part == (0 if is_early(b, q + 1) else 1):
                        transpose_chunks(b, q + 1, 0)
                        if is_early(b, q + 1):
                            transpose_chunks(b, q + 1, 2)
                    if has(b, q, -1):
                        output(b, q - 1, part)
                    if has(b, q, 1) and part == 1:
                        lo_part(b, q + 1, 0)
                        if not is_early(b, q + 1):
                            transpose_chunks(b, q + 1, 2)
                    if has(b, q, 1) and part == 2:
                        lo_part(b, q + 1, 2)
                    if part == variances_after(b, q):
                        add_eps(b, q - q % 2 + 2)
                    if isinstance(b, int) and b + q + 1 < GROUPS and part == (0 if b + q else 3):
                        transpose_mem(q + 1)

            split_w_lif(range(0, 2))
            add_eps(0, 0, 1)
            split_w_lif(range(2, C))
            transpose_chunks(0, 0, 0)
            transpose_chunks(0, 0, 2)
            add_eps(0, 1, 1)
            lo_part(0, 0, 0)
            lo_part(0, 0, 2)
            transpose_mem(0)
            dve.wait_ge(w_rec_loaded, 16 * Q)
            for k in range(C):
                nc.vector.tensor_copy(wr[:, 0, k, :], raw_w_rec[:, k, :]).then_inc(wr_hi_ready, 1)
            for q in range(LOOP_FIRST):
                step(0, q)
            with dve.Fori(0, LOOPS) as i:
                for q in range(LOOP_FIRST, LOOP_FIRST + SLOTS):
                    step(i * SLOTS, q)
            for q in range(LOOP_FIRST, LAST_Q + 1):
                step(LOOP_END, q)

        @block.tensor
        def _(pe):
            def means(b, q, n=2):
                pe.wait_ge(sum_ready, b + q + n)
                if has(b, q, -1):
                    pe.wait_ge(var_eps_ready, b + q)
                cols = slice(q % 2, q % 2 + n)
                nc.tensor.matmul(stat_ps[:, cols], averaging[:], sums[:, cols], start=True, stop=True).then_inc(mean_ready, n)

            def variances(b, q, n=2):
                pe.wait_ge(squares_ready, b + q + n)
                nc.tensor.matmul(stat_ps[:, 2 + q % 2:2 + q % 2 + n], averaging[:], squares[:, q % 2:q % 2 + n],
                                 start=True, stop=True).then_inc(var_ready, n)

            def lif_product(b, q, e):
                if has(b, q, -1) or e >= 2:
                    pe.wait_ge(u_ready, (b + q) * C + e - 1)
                hi, lo = xT[q % 2][:, 0], xT[q % 2][:, 1]
                cols = slice(e * P, (e + 1) * P)
                for k in range(C):
                    if e == 0 and k % 2 == 0:
                        pe.wait_ge(lo_ready, (b + q) * C + k + 2)
                    nc.tensor.matmul(y_ps[e % 2][:], wl[:, 1, k, cols], hi[:, k, :], start=k == 0, stop=False)
                    nc.tensor.matmul(y_ps[e % 2][:], wl[:, 0, k, cols], lo[:, k, :], start=False, stop=False)
                    last = nc.tensor.matmul(y_ps[e % 2][:], wl[:, 0, k, cols], hi[:, k, :], start=False, stop=k == C - 1)
                last.then_inc(y_ready, 1)

            def rec_product(b, q, j):
                if j == 0:
                    pe.wait_ge(gated_ready, (b + q) * C + C)
                if has(b, q, -1) or j >= 2:
                    pe.wait_ge(out_ready, (b + q) * TPP + j - 1)
                hi, lo = gated[q % 2][:, 0], gated[q % 2][:, 1]
                cols = slice(j * P, (j + 1) * P)
                for k in range(C):
                    nc.tensor.matmul(r_ps[:, j % 2, :], lo[:, k, cols], wr[:, 0, k, :], start=k == 0, stop=False)
                    nc.tensor.matmul(r_ps[:, j % 2, :], hi[:, k, cols], wr[:, 1, k, :], start=False, stop=False)
                    last = nc.tensor.matmul(r_ps[:, j % 2, :], hi[:, k, cols], wr[:, 0, k, :], start=False, stop=k == C - 1)
                last.then_inc(r_ready, 1)

            def step(b, q):
                for part in range(4):
                    if has(b, q, 0):
                        lif_product(b, q, part)
                    if has(b, q, -1):
                        rec_product(b, q - 1, part)
                    if starts_pair(b, q) and part == 1:
                        means(b, q + 2)
                    if part == variances_after(b, q):
                        variances(b, q - q % 2 + 2)

            pe.wait_ge(averaging_ready, 1)
            for q in range(2):
                means(0, q, 1)
                variances(0, q, 1)
            pe.wait_ge(wl_ready, C)
            step(0, 0)
            pe.wait_ge(wr_ready, C)
            for q in range(1, LOOP_FIRST):
                step(0, q)
            with pe.Fori(0, LOOPS) as i:
                for q in range(LOOP_FIRST, LOOP_FIRST + SLOTS):
                    step(i * SLOTS, q)
            for q in range(LOOP_FIRST, LAST_Q + 1):
                step(LOOP_END, q)


_INS = ["x", "L0_conv_tr_mx", "L0_conv_W_lif", "L0_conv_b_lif", "L0_conv_W_rec", "L0_conv_b_rec"]


def kernel(**inputs):
    import numpy as _np
    import concourse.bacc as _bacc
    from concourse import mybir as _mybir
    from concourse.bass_utils import run_bass_kernel_spmd as _run

    nc = _bacc.Bacc("TRN2", target_bir_lowering=False, num_devices=1)
    arrays, args = {}, []
    for name in _INS:
        a = _np.ascontiguousarray(inputs[name])
        arrays[f"in_{name}_dram"] = a
        args.append(nc.dram_tensor(f"in_{name}_dram", a.shape, _mybir.dt.from_np(a.dtype), kind="ExternalInput").ap())
    out_shape = arrays["in_x_dram"].shape
    args.append(nc.dram_tensor("out_0_dram", out_shape, _mybir.dt.float32, kind="ExternalOutput").ap())
    lif_block(nc, *args)
    r = _run(nc, [arrays], core_ids=[0])
    return r.results[0]["out_0_dram"]
```
